# Optimizing a Trainium2 kernel written in Bass

```python
import numpy as np
import jax
import jax.numpy as jnp

def _softmax(x, axis=-1):
    return jax.nn.softmax(x, axis=axis)

def _gelu(x):
    return jax.nn.gelu(x, approximate=True)

def _silu(x):
    return jax.nn.silu(x)

def _sigmoid(x):
    return jax.nn.sigmoid(x)

def _layernorm(x, axis=-1, eps=1e-05):
    m = jnp.mean(x, axis=axis, keepdims=True)
    v = jnp.var(x, axis=axis, keepdims=True)
    return (x - m) / jnp.sqrt(v + eps)

def _scatter_add(tgt, idx, src, axis=0):
    return tgt.at[idx].add(src)

def _segment_sum(src, seg, n):
    return jax.ops.segment_sum(src, seg, n)
kernel_name = 'mk_adaln_ffn_d1_seqx_r8_cbd707'

def setup_inputs(seed: int=0):
    np.random.seed(seed)
    _w = jnp.asarray

    def _rec_inputs():
        import jax
        import jax.numpy as jnp
        _rk = jax.random.key(seed)
        x = -0.000125 + 0.9999 * jax.random.normal(jax.random.fold_in(_rk, 1), (32, 32, 256), jnp.float32)
        _lenS = 32 - jax.random.randint(jax.random.fold_in(_rk, 7), (32,), 0, max(1, 32 // 4) + 1, jnp.int32)
        _lenS2 = 32 - jax.random.randint(jax.random.fold_in(_rk, 8), (32,), 0, max(1, 32 // 4) + 1, jnp.int32)
        itok_B_0_7 = jax.random.randint(jax.random.fold_in(_rk, 11), (32,), 0, 8, jnp.int32)
        fside_8xS_0 = -0.00162727 + 0.0609077 * jax.random.normal(jax.random.fold_in(_rk, 12), (8, 32), jnp.float32)
        return (x, itok_B_0_7, fside_8xS_0)
    x, itok_B_0_7, fside_8xS_0 = _rec_inputs()

    def _L0_cond_setup():
        import jax, jax.numpy as jnp
        import numpy as np
        B, C, T = (64, 32, 256)
        D, N = (32, 8)
        key = jax.random.key(seed)
        k_x, k_s, k_w, k_b = jax.random.split(key, 4)
        scale = 1.0 / np.sqrt(C)
        x = jax.random.normal(k_x, (B, C, T), dtype=jnp.float32)
        subjects = jax.random.randint(k_s, (B,), 0, N, dtype=jnp.int64)
        weights = jax.random.normal(k_w, (N, C, D), dtype=jnp.float32) * scale
        bias = jax.random.normal(k_b, (N, D), dtype=jnp.float32) * scale
        return {'x': x, 'subjects': subjects, 'weights': weights, 'bias': bias}
    _L0_cond_all = _L0_cond_setup()
    _L0_cond_in = {k: v for k, v in _L0_cond_all.items() if k in ('weights',)}
    del _L0_cond_all

    def _L0_ffn_setup():
        import jax, jax.numpy as jnp
        import numpy as np
        B, S, H, I = (1, 64, 256, 768)

        def _quantized_matmul(x, w, scale):
            wq = w.astype(jnp.float8_e4m3fn).astype(x.dtype)
            y = jnp.einsum('bsi,io->bso', x, wq)
            return y * scale
        key = jax.random.key(seed)
        ks = jax.random.split(key, 7)
        return {'x': jax.random.normal(ks[0], (B, S, H), dtype=jnp.float32), 'gate_w': jax.random.normal(ks[1], (H, I), dtype=jnp.float32) * 0.02, 'up_w': jax.random.normal(ks[2], (H, I), dtype=jnp.float32) * 0.02, 'down_w': jax.random.normal(ks[3], (I, H), dtype=jnp.float32) * 0.02, 'gate_scale': jax.random.uniform(ks[4], (I,), dtype=jnp.float32, minval=0.5, maxval=1.5), 'up_scale': jax.random.uniform(ks[5], (I,), dtype=jnp.float32, minval=0.5, maxval=1.5), 'down_scale': jax.random.uniform(ks[6], (H,), dtype=jnp.float32, minval=0.5, maxval=1.5)}
    _L0_ffn_all = _L0_ffn_setup()
    _L0_ffn_in = {k: v for k, v in _L0_ffn_all.items() if k in ('gate_w', 'up_w', 'down_w', 'gate_scale', 'up_scale', 'down_scale')}
    del _L0_ffn_all
    return {'x': x, 'itok_B_0_7': itok_B_0_7, 'fside_8xS_0': fside_8xS_0, 'L0_cond_weights': _L0_cond_in['weights'], 'L0_ffn_gate_w': _L0_ffn_in['gate_w'], 'L0_ffn_up_w': _L0_ffn_in['up_w'], 'L0_ffn_down_w': _L0_ffn_in['down_w'], 'L0_ffn_gate_scale': _L0_ffn_in['gate_scale'], 'L0_ffn_up_scale': _L0_ffn_in['up_scale'], 'L0_ffn_down_scale': _L0_ffn_in['down_scale']}

def reference(x, itok_B_0_7, fside_8xS_0, L0_cond_weights, L0_ffn_gate_w, L0_ffn_up_w, L0_ffn_down_w, L0_ffn_gate_scale, L0_ffn_up_scale, L0_ffn_down_scale):
    import jax
    import jax.numpy as jnp

    def _L0_cond_ref(x, subjects, weights, bias):
        import jax, jax.numpy as jnp
        import numpy as np
        B, C, T = (64, 32, 256)
        D, N = (32, 8)
        w = weights[subjects]
        b = bias[subjects]
        out = jnp.einsum('bct,bcd->bdt', x, w)
        out = out + b[:, :, None]
        return out

    def _L0_ffn_ref(x, gate_w, up_w, down_w, gate_scale, up_scale, down_scale):
        import jax, jax.numpy as jnp
        import numpy as np
        B, S, H, I = (1, 64, 256, 768)

        def _quantized_matmul(x, w, scale):
            wq = w.astype(jnp.float8_e4m3fn).astype(x.dtype)
            y = jnp.einsum('bsi,io->bso', x, wq)
            return y * scale
        gate = jax.nn.silu(_quantized_matmul(x, gate_w, gate_scale))
        up = _quantized_matmul(x, up_w, up_scale)
        fuse = gate * up
        return _quantized_matmul(fuse, down_w, down_scale)
    x = x + _L0_ffn_ref(_L0_cond_ref(x, itok_B_0_7, L0_cond_weights, fside_8xS_0), L0_ffn_gate_w, L0_ffn_up_w, L0_ffn_down_w, L0_ffn_gate_scale, L0_ffn_up_scale, L0_ffn_down_scale)
    return x

_drawn_inputs = setup_inputs


def setup_inputs(seed=0):
    import zlib

    import numpy as np

    out = dict(_drawn_inputs(seed))
    spreads = {}
    factors = {'fside_8xS_0': 8.0,
     'L0_ffn_gate_scale': 5.005,
     'L0_ffn_up_scale': 5.915,
     'L0_ffn_down_scale': 5.704}
    for name, (base, spread) in spreads.items():
        noise = np.random.default_rng([zlib.crc32(name.encode()), seed]).standard_normal(out[name].shape)
        drawn = base * np.exp(spread * noise) if base else spread * noise
        out[name] = jnp.asarray(drawn.astype(out[name].dtype))
    for name, factor in factors.items():
        out[name] = (out[name] * factor).astype(out[name].dtype)
    return out
```

```python
from contextlib import ExitStack

import concourse.bass as bass
from concourse import mybir

ALU = mybir.AluOpType
ACT = mybir.ActivationFunctionType
F32 = mybir.dt.float32
F32R = mybir.dt.float32r
I32 = mybir.dt.int32
U32 = mybir.dt.uint32

P = 128


def adaln_ffn(
    nc: bass.Bass,
    x: bass.AP,
    subjects: bass.AP,
    bias: bass.AP,
    cond_w: bass.AP,
    gate_w: bass.AP,
    up_w: bass.AP,
    down_w: bass.AP,
    gate_scale: bass.AP,
    up_scale: bass.AP,
    down_scale: bass.AP,
    out: bass.AP,
):
    B, C, T = x.shape
    N, _, D = cond_w.shape
    HID = gate_w.shape[1]
    J = P // C
    G = B // J
    KC = T // P
    IC = HID // P
    HALVES = 2
    TOK = B * D // HALVES
    GH = G // HALVES
    GU = 2 * KC * P
    WCOL = GU + T
    STEPS = IC * HALVES
    LAG = 2
    assert C == D and TOK == 512 and B * C == G * P

    EXPONENT = 0x7F800000
    HALF_MORE = 0x00400000
    LEAST = 1.5 * 2.0 ** -6
    SHIFT = 2.0 ** (23 - 3)

    x_rows = x.rearrange("(g j) c t -> (j c) g t", j=J)
    out_rows = out.rearrange("(g j) c t -> (j c) g t", j=J)
    cond_rows = cond_w.rearrange("n c d -> c n d")
    gate_rows = gate_w.rearrange("(k p) i -> p k i", p=P)
    up_rows = up_w.rearrange("(k p) i -> p k i", p=P)
    down_rows = down_w.rearrange("(q p) t -> q p t", p=P)

    with ExitStack() as ctx:
        def sb(name, shape, dt=F32):
            return ctx.enter_context(nc.sbuf_tensor(name, shape, dt))

        def ps(name, shape):
            return ctx.enter_context(nc.psum_tensor(name, shape, F32))

        def sem(name):
            return ctx.enter_context(nc.semaphore(name))

        x_sb = sb("x_sb", [P, G, T])
        subj_i = sb("subj_i", [P, B], I32)
        cond_rep = sb("cond_rep", [P, N, D])
        bias_in = sb("bias_in", [64, D])
        bias_hl = sb("bias_hl", [64, D], F32R)
        scale_in = sb("scale_in", [2 * IC, P])
        scale_col = sb("scale_col", [P, 2 * IC])
        down_sc = sb("down_sc", [P, T])
        w_in = sb("w_in", [P, IC, WCOL])
        w_big = sb("w_big", [P, WCOL])
        w_sum = sb("w_sum", [P, WCOL])
        w_q = sb("w_q", [P, IC, WCOL], F32R)
        subj_f = sb("subj_f", [P, B])
        subj_g = sb("subj_g", [P, G])
        iota_n = sb("iota_n", [P, N])
        iota_p = sb("iota_p", [64, 1])
        ident = sb("ident", [2 * IC, 2 * IC])
        ones_f = sb("ones_f", [64, P])
        ones_r = sb("ones_r", [64, P], F32R)
        pick = sb("pick", [P, N, G], U32)
        cond_g = sb("cond_g", [P, G, D])
        cond_bd = sb("cond_bd", [P, G, P])
        bias_tok = sb("bias_tok", [64, B, D], F32R)
        h_hi = sb("h_hi", [P, HALVES, KC, TOK], F32R)
        h_lo = sb("h_lo", [P, HALVES, KC, TOK], F32R)
        silu = sb("silu", [P, 2, TOK])
        fuse = sb("fuse", [P, 2, TOK])
        f_hi = sb("f_hi", [P, LAG + 1, TOK], F32R)
        f_lo = sb("f_lo", [P, LAG + 1, TOK], F32R)
        y_sc = sb("y_sc", [P, G, T])
        res = sb("res", [P, G, T])

        acc = ps("acc", [P, 4, 512])
        gu = ps("gu", [P, 2, 2, 512])
        scale_ps = gu[:, 1, 0, 0:2 * IC]

        subj_in = sem("subj_in")
        cond_in = sem("cond_in")
        bias_ld = sem("bias_ld")
        scale_ld = sem("scale_ld")
        down_sc_ld = sem("down_sc_ld")
        x_ld = [sem(f"x_ld{n}") for n in range(HALVES)]
        gu_ld = [sem(f"gu_ld{i}") for i in range(IC)]
        down_ld = [sem(f"down_ld{i}") for i in range(IC)]
        bias_zeroed = sem("bias_zeroed")
        ident_zeroed = sem("ident_zeroed")
        iota_made = sem("iota_made")
        ident_made = sem("ident_made")
        ones_set = sem("ones_set")
        consts_made = sem("consts_made")
        subj_float = sem("subj_float")
        subj_placed = sem("subj_placed")
        picks_made = sem("picks_made")
        cond_picked = sem("cond_picked")
        cond_placed = sem("cond_placed")
        bias_round = sem("bias_round")
        bias_split = sem("bias_split")
        bias_made = sem("bias_made")
        ones_made = sem("ones_made")
        scale_tp = sem("scale_tp")
        scales_made = sem("scales_made")
        h_made = sem("h_made")
        h_hi_made = sem("h_hi_made")
        h_lo_made = sem("h_lo_made")
        quant_power = sem("quant_power")
        quant_big = sem("quant_big")
        quant_sum = sem("quant_sum")
        quant_done = sem("quant_done")
        gate_made = sem("gate_made")
        up_made = sem("up_made")
        silu_made = sem("silu_made")
        fuse_made = sem("fuse_made")
        f_hi_made = sem("f_hi_made")
        f_lo_made = sem("f_lo_made")
        down_made = sem("down_made")
        y_scaled = sem("y_scaled")
        res_made = sem("res_made")
        stored = sem("stored")

        block = ctx.enter_context(nc.Block())

        @block.sync
        def _(sp):
            sp.dma_start(subj_i[:], subjects.partition_broadcast(P)).then_inc(subj_in, 16)
            for j in range(J):
                sp.dma_start(cond_rep[j * C:(j + 1) * C], cond_rows).then_inc(cond_in, 16)
            sp.dma_start(x_sb[:, 0:GH], x_rows[:, 0:GH]).then_inc(x_ld[0], 16)
            sp.dma_start(x_sb[:, GH:G], x_rows[:, GH:G]).then_inc(x_ld[1], 16)
            for i in range(1, IC):
                cols = slice(i * P, (i + 1) * P)
                for part, rows in ((0, gate_rows), (1, up_rows)):
                    dst = w_in[:, i, part * KC * P:(part + 1) * KC * P].rearrange("p (k c) -> p k c", k=KC)
                    sp.dma_start(dst, rows[:, :, cols]).then_inc(gu_ld[i], 16)
                sp.dma_start(w_in[:, i, GU:WCOL], down_rows[i]).then_inc(down_ld[i], 16)
            for m in range(0, G, 2):
                sp.wait_ge(res_made, m + 2)
                sp.dma_start(out_rows[:, m:m + 2], res[:, m:m + 2]).then_inc(stored, 16)
            sp.wait_ge(stored, 16 * G // 2)

        @block.scalar
        def _(act):
            for part, rows in ((0, gate_rows), (1, up_rows)):
                dst = w_in[:, 0, part * KC * P:(part + 1) * KC * P].rearrange("p (k c) -> p k c", k=KC)
                act.dma_start(dst, rows[:, :, 0:P]).then_inc(gu_ld[0], 16)
            act.wait_ge(bias_zeroed, 1)
            for q in range(2):
                act.dma_start(bias_in[32 * q:32 * q + N], bias).then_inc(bias_ld, 16)
            act.dma_start(scale_in[0:IC], gate_scale.rearrange("(q p) -> q p", p=P)).then_inc(scale_ld, 16)
            act.dma_start(scale_in[IC:2 * IC], up_scale.rearrange("(q p) -> q p", p=P)).then_inc(scale_ld, 16)
            act.dma_start(w_in[:, 0, GU:WCOL], down_rows[0]).then_inc(down_ld[0], 16)
            act.dma_start(down_sc[:], down_scale.partition_broadcast(P)).then_inc(down_sc_ld, 16)
            act.wait_ge(cond_picked, N)
            act.wait_ge(consts_made, 1)
            for j in range(0, 2):
                rows = slice(j * C, (j + 1) * C)
                nc.scalar.copy(cond_bd[rows, :, j * D:(j + 1) * D], cond_g[rows]).then_inc(cond_placed, 1)
            act.wait_ge(scale_tp, 1)
            nc.scalar.copy(scale_col[:], scale_ps).then_inc(scales_made, 1)
            for n in range(HALVES):
                for k in range(KC):
                    act.wait_ge(h_made, KC * n + k + 1)
                    nc.scalar.copy(h_hi[:, n, k], acc[:, KC * n + k]).then_inc(h_hi_made, 1)
            act.wait_ge(scales_made, 1)

            def silu_of(s):
                act.wait_ge(gate_made, s + 1)
                if s >= 2:
                    act.wait_ge(fuse_made, s - 1)
                nc.scalar.activation(silu[:, s % 2], gu[:, s % 2, 0], ACT.Silu,
                                     scale=scale_col[:, s // 2:s // 2 + 1]).then_inc(silu_made, 1)

            def round_of(s):
                act.wait_ge(fuse_made, s + 1)
                if s > LAG:
                    act.wait_ge(down_made, s - LAG)
                nc.scalar.copy(f_hi[:, s % (LAG + 1)], fuse[:, s % 2]).then_inc(f_hi_made, 1)

            for s in range(STEPS):
                silu_of(s)
                if s >= 1:
                    round_of(s - 1)
            round_of(STEPS - 1)

        @block.gpsimd
        def _(pool):
            nc.gpsimd.memset(bias_in[:], 0.0).then_inc(bias_zeroed, 1)
            pool.wait_ge(bias_zeroed, 1)
            nc.gpsimd.iota(iota_n[:], [[1, N]], base=0, channel_multiplier=0,
                           allow_small_or_imprecise_dtypes=True).then_inc(iota_made, 1)
            pool.wait_ge(iota_made, 1)
            for q in range(2):
                nc.gpsimd.iota(iota_p[32 * q:32 * q + 32], [[0, 1]], base=0, channel_multiplier=1,
                               allow_small_or_imprecise_dtypes=True).then_inc(iota_made, 1)
                pool.wait_ge(iota_made, q + 2)
            nc.gpsimd.memset(ident[:], 0.0).then_inc(ident_zeroed, 1)
            pool.wait_ge(ident_zeroed, 1)
            nc.gpsimd.affine_select(out=ident[:], in_=ident[:], compare_op=ALU.not_equal, fill=1.0, base=0,
                                    pattern=[[-1, 2 * IC]], channel_multiplier=1).then_inc(ident_made, 1)
            pool.wait_ge(ident_made, 1)
            nc.gpsimd.memset(ones_f[:], 1.0).then_inc(ones_set, 1)
            pool.wait_ge(ones_set, 1)
            nc.gpsimd.memset(cond_bd[:], 0.0).then_inc(consts_made, 1)

            for m in range(G):
                pool.wait_ge(x_ld[m // GH], 16)
                pool.wait_ge(y_scaled, m + 1)
                nc.gpsimd.tensor_tensor(res[:, m], y_sc[:, m], x_sb[:, m], ALU.add).then_inc(res_made, 1)

        @block.vector
        def _(dve):
            def powers(i, lo, hi):
                nc.vector.tensor_scalar(w_big[:, lo:hi].bitcast(U32), w_in[:, i, lo:hi].bitcast(U32), EXPONENT,
                                        HALF_MORE, ALU.bitwise_and, ALU.bitwise_or).then_inc(quant_power, 1)

            def quantise(i, lo, hi, c, ld):
                dve.wait_ge(ld[i], 32 if ld is gu_ld else 16)
                if c >= 1:
                    dve.wait_ge(quant_done, c)
                powers(i, lo, hi)
                dve.wait_ge(quant_power, c + 1)
                nc.vector.tensor_scalar(w_big[:, lo:hi], w_big[:, lo:hi], LEAST, SHIFT,
                                        ALU.max, ALU.mult).then_inc(quant_big, 1)
                dve.wait_ge(quant_big, c + 1)
                nc.vector.tensor_tensor(w_sum[:, lo:hi], w_in[:, i, lo:hi], w_big[:, lo:hi],
                                        ALU.add).then_inc(quant_sum, 1)
                dve.wait_ge(quant_sum, c + 1)
                nc.vector.tensor_tensor(w_q[:, i, lo:hi], w_sum[:, lo:hi], w_big[:, lo:hi],
                                        ALU.subtract).then_inc(quant_done, 1)

            dve.wait_ge(subj_in, 16)
            nc.vector.tensor_copy(subj_f[:], subj_i[:]).then_inc(subj_float, 1)
            dve.wait_ge(subj_float, 1)
            for j in range(J):
                rows = slice(j * C, (j + 1) * C)
                nc.vector.tensor_copy(subj_g[rows], subj_f[rows].rearrange("p (g j) -> p g j", j=J)[:, :, j]
                                      ).then_inc(subj_placed, 1)
            dve.wait_ge(subj_placed, J)
            dve.wait_ge(consts_made, 1)
            nc.vector.tensor_tensor(pick[:], subj_g[:].unsqueeze(1).to_broadcast([P, N, G]),
                                    iota_n[:].unsqueeze(2).to_broadcast([P, N, G]),
                                    ALU.is_equal).then_inc(picks_made, 1)
            dve.wait_ge(picks_made, 1)
            dve.wait_ge(cond_in, 16 * J)
            for n in range(N):
                data = cond_rep[:, n].unsqueeze(1).to_broadcast([P, G, D])
                if n == 0:
                    nc.vector.tensor_copy(cond_g[:], data).then_inc(cond_picked, 1)
                else:
                    dve.wait_ge(cond_picked, n)
                    nc.vector.copy_predicated(cond_g[:], pick[:, n].unsqueeze(2).to_broadcast([P, G, D]),
                                              data).then_inc(cond_picked, 1)
            dve.wait_ge(cond_picked, N)
            for j in range(2, J):
                rows = slice(j * C, (j + 1) * C)
                nc.vector.tensor_copy(cond_bd[rows, :, j * D:(j + 1) * D], cond_g[rows]).then_inc(cond_placed, 1)

            nc.vector.tensor_copy(ones_r[:], ones_f[:]).then_inc(ones_made, 1)
            dve.wait_ge(bias_ld, 32)
            nc.vector.tensor_copy(bias_hl[:], bias_in[:]).then_inc(bias_round, 1)
            dve.wait_ge(bias_round, 1)
            nc.vector.tensor_tensor(bias_hl[32:64], bias_in[32:64], bias_hl[32:64].bitcast(F32),
                                    ALU.subtract).then_inc(bias_split, 1)
            dve.wait_ge(bias_split, 1)
            nc.vector.scalar_tensor_tensor(
                bias_tok[:], subj_f[0:64].unsqueeze(2).to_broadcast([64, B, D]), iota_p[:],
                bias_hl[:].bitcast(F32).unsqueeze(1).to_broadcast([64, B, D]),
                ALU.is_equal, ALU.mult).then_inc(bias_made, 1)

            quantise(0, 0, GU, 0, gu_ld)

            for n in range(HALVES):
                for k in range(KC):
                    dve.wait_ge(h_hi_made, KC * n + k + 1)
                    nc.vector.tensor_tensor(h_lo[:, n, k], acc[:, KC * n + k], h_hi[:, n, k].bitcast(F32),
                                            ALU.subtract).then_inc(h_lo_made, 1)
            quantise(0, GU, WCOL, 1, down_ld)

            def rest_of(s):
                dve.wait_ge(f_hi_made, s + 1)
                if s > LAG:
                    dve.wait_ge(down_made, s - LAG)
                nc.vector.tensor_tensor(f_lo[:, s % (LAG + 1)], fuse[:, s % 2],
                                        f_hi[:, s % (LAG + 1)].bitcast(F32),
                                        ALU.subtract).then_inc(f_lo_made, 1)

            dve.wait_ge(scales_made, 1)
            c = 2
            for s in range(STEPS):
                i = s // 2 + 1
                if i < IC:
                    if s % 2 == 0:
                        quantise(i, 0, GU, c, gu_ld)
                    else:
                        quantise(i, GU, WCOL, c, down_ld)
                    c += 1
                dve.wait_ge(up_made, s + 1)
                dve.wait_ge(silu_made, s + 1)
                if s >= 2:
                    dve.wait_ge(f_lo_made, s - 1)
                nc.vector.scalar_tensor_tensor(
                    fuse[:, s % 2], gu[:, s % 2, 1], scale_col[:, IC + s // 2:IC + s // 2 + 1], silu[:, s % 2],
                    ALU.mult, ALU.mult).then_inc(fuse_made, 1)
                if s >= 1:
                    rest_of(s - 1)
            rest_of(STEPS - 1)

            dve.wait_ge(down_sc_ld, 16)
            for m in range(G):
                dve.wait_ge(down_made, STEPS - HALVES + m // GH + 1)
                nc.vector.tensor_tensor(y_sc[:, m], acc[:, m // 2, (m % 2) * T:(m % 2 + 1) * T], down_sc[:],
                                        ALU.mult).then_inc(y_scaled, 1)

        @block.tensor
        def _(pe):
            pe.wait_ge(consts_made, 1)
            pe.wait_ge(scale_ld, 32)
            nc.tensor.matmul(scale_ps, scale_in[:], ident[:], start=True, stop=True).then_inc(scale_tp, 1)

            pe.wait_ge(cond_placed, J)
            pe.wait_ge(ones_made, 1)
            pe.wait_ge(bias_made, 1)
            for n in range(HALVES):
                pe.wait_ge(x_ld[n], 16)
                for k in range(KC):
                    bank = acc[:, KC * n + k]
                    for g in range(GH):
                        nc.tensor.matmul(bank[:, g * P:(g + 1) * P], x_sb[:, n * GH + g, k * P:(k + 1) * P],
                                         cond_bd[:, n * GH + g], start=(g == 0), stop=False,
                                         skip_group_check=True)
                    nc.tensor.matmul(bank, ones_r[:], bias_tok[:, n * TOK // D:(n + 1) * TOK // D], start=False,
                                     stop=True, skip_group_check=True).then_inc(h_made, 1)

            def gate_up(s):
                i, n = divmod(s, 2)
                if s >= 2:
                    pe.wait_ge(silu_made, s - 1)
                pe.wait_ge(quant_done, 2 * i + 1 if i else 1)
                for part, made in ((0, gate_made), (1, up_made)):
                    if part == 1 and s >= 2:
                        pe.wait_ge(fuse_made, s - 1)
                    if s == 1 and part == 0:
                        pe.wait_ge(scales_made, 1)
                    for v, (h, h_sem) in enumerate(((h_hi, h_hi_made), (h_lo, h_lo_made))):
                        for k in range(KC):
                            if s < 2 and part == 0:
                                pe.wait_ge(h_sem, KC * n + k + 1)
                            col = (part * KC + k) * P
                            last = nc.tensor.matmul(gu[:, s % 2, part], w_q[:, i, col:col + P], h[:, n, k],
                                                    start=(v == 0 and k == 0), stop=(v == 1 and k == KC - 1))
                    last.then_inc(made, 1)

            def down(s):
                i, n = divmod(s, 2)
                pe.wait_ge(quant_done, 2 * i + 2)
                for v, (f, f_sem) in enumerate(((f_hi, f_hi_made), (f_lo, f_lo_made))):
                    pe.wait_ge(f_sem, s + 1)
                    if s < 2:
                        pe.wait_ge(h_lo_made, KC * (n + 1))
                    for m in range(GH):
                        tile = n * GH + m
                        last = nc.tensor.matmul(acc[:, tile // 2, (tile % 2) * T:(tile % 2 + 1) * T],
                                                f[:, s % (LAG + 1), m * P:(m + 1) * P], w_q[:, i, GU:WCOL],
                                                start=(i == 0 and v == 0 and tile % 2 == 0),
                                                stop=(i == IC - 1 and v == 1), skip_group_check=True)
                last.then_inc(down_made, 1)

            for s in range(STEPS):
                gate_up(s)
                if s >= LAG:
                    down(s - LAG)
            for s in range(STEPS - LAG, STEPS):
                down(s)


_INS = ["x", "itok_B_0_7", "fside_8xS_0", "L0_cond_weights", "L0_ffn_gate_w", "L0_ffn_up_w", "L0_ffn_down_w",
        "L0_ffn_gate_scale", "L0_ffn_up_scale", "L0_ffn_down_scale"]


def kernel(**inputs):
    import numpy as _np
    import concourse.bacc as _bacc
    from concourse import mybir as _mybir
    from concourse.bass_utils import run_bass_kernel_spmd as _run

    nc = _bacc.Bacc("TRN2", target_bir_lowering=False, num_devices=1)
    arrays, args = {}, []
    for name in _INS:
        a = _np.ascontiguousarray(inputs[name])
        arrays[f"in_{name}_dram"] = a
        args.append(nc.dram_tensor(f"in_{name}_dram", a.shape, _mybir.dt.from_np(a.dtype), kind="ExternalInput").ap())
    shape = arrays["in_x_dram"].shape
    args.append(nc.dram_tensor("out_0_dram", shape, _mybir.dt.float32, kind="ExternalOutput").ap())
    adaln_ffn(nc, *args)
    r = _run(nc, [arrays], core_ids=[0])
    return r.results[0]["out_0_dram"]
```

```python
from contextlib import ExitStack

import concourse.bass as bass
from concourse import mybir

ALU = mybir.AluOpType
ACT = mybir.ActivationFunctionType
BF16 = mybir.dt.bfloat16
F32 = mybir.dt.float32
F32R = mybir.dt.float32r
I32 = mybir.dt.int32
U32 = mybir.dt.uint32

P = 128


def adaln_ffn(
    nc: bass.Bass,
    x: bass.AP,
    subjects: bass.AP,
    bias: bass.AP,
    cond_w: bass.AP,
    gate_w: bass.AP,
    up_w: bass.AP,
    down_w: bass.AP,
    gate_scale: bass.AP,
    up_scale: bass.AP,
    down_scale: bass.AP,
    out: bass.AP,
):
    B, C, T = x.shape
    N, _, D = cond_w.shape
    HID = gate_w.shape[1]
    J = P // C
    G = B // J
    KC = T // P
    IC = HID // P
    HALVES = 2
    TOK = B * D // HALVES
    GH = G // HALVES
    GU = 2 * KC * P
    WCOL = GU + T
    STEPS = IC * HALVES
    LAG = 2
    SLOTS = 4
    EARLY = 2
    LAST = 2
    WARM = (8, 9)
    DOWN_LOADS = ((0, 1), (1, 2), (2, IC))
    STEP = [(i, n) for i in range(IC - 3) for n in range(HALVES)] + [(i, n) for n in range(HALVES)
                                                                     for i in range(IC - 3, IC)]
    HALF_DONE = [max(s for s, (_, m) in enumerate(STEP) if m == n) for n in range(HALVES)]
    assert C == D and TOK == 512 and B * C == G * P

    EXPONENT = 0x7F800000
    HALF_MORE = 0x00400000
    LEAST = 1.5 * 2.0 ** -6
    SHIFT = 2.0 ** (23 - 3)

    x_rows = x.rearrange("(g j) c t -> (j c) g t", j=J)
    out_rows = out.rearrange("(g j) c t -> (j c) g t", j=J)
    cond_rows = cond_w.rearrange("n c d -> c n d")
    gate_rows = gate_w.rearrange("(k p) i -> p k i", p=P)
    up_rows = up_w.rearrange("(k p) i -> p k i", p=P)
    down_rows = down_w.rearrange("(q p) t -> p q t", p=P)

    with ExitStack() as ctx:
        def sb(name, shape, dt=F32):
            return ctx.enter_context(nc.sbuf_tensor(name, shape, dt))

        def ps(name, shape):
            return ctx.enter_context(nc.psum_tensor(name, shape, F32))

        def sem(name):
            return ctx.enter_context(nc.semaphore(name))

        x_sb = sb("x_sb", [P, G, T])
        subj_i = sb("subj_i", [P, B], I32)
        cond_rep = sb("cond_rep", [P, N, D])
        bias_in = sb("bias_in", [N, D])
        scale_in = sb("scale_in", [2 * IC, P])
        scale_col = sb("scale_col", [P, 2 * IC])
        down_sc = sb("down_sc", [P, T])
        w_in = sb("w_in", [P, IC, WCOL])
        w_big = sb("w_big", [P, IC, WCOL])
        w_q = sb("w_q", [P, IC, WCOL], F32R)
        subj_f = sb("subj_f", [P, B])
        subj_g = sb("subj_g", [P, G])
        iota_n = sb("iota_n", [P, N])
        iota_p = sb("iota_p", [N, 1])
        big_least = sb("big_least", [P, 1])
        ident = sb("ident", [2 * IC, 2 * IC])
        warm = sb("warm", [P, TOK], BF16)
        ones_f = sb("ones_f", [2, P])
        ones_r = sb("ones_r", [2, P], F32R)
        pick = sb("pick", [P, N, G], U32)
        pick_b = sb("pick_b", [N, B])
        cond_g = sb("cond_g", [P, G, D])
        cond_bd = sb("cond_bd", [P, G, P])
        bias_b = sb("bias_b", [B, 2, D], F32R)
        bias_tok = sb("bias_tok", [2, B, D], F32R)
        h_hi = sb("h_hi", [P, HALVES, KC, TOK], F32R)
        h_lo = sb("h_lo", [P, HALVES, KC, TOK], F32R)
        silu = sb("silu", [P, 2, TOK])
        fuse = sb("fuse", [P, SLOTS, TOK])
        f_hi = sb("f_hi", [P, SLOTS, TOK], F32R)
        f_lo = sb("f_lo", [P, SLOTS, TOK], F32R)
        y_sc = sb("y_sc", [P, G, T])
        res = sb("res", [P, G, T])

        acc = ps("acc", [P, 4, 512])
        gu = ps("gu", [P, 2, 2, 512])
        warm_ps = gu[:, 0, 0]
        scale_ps = gu[:, 1, 0, 0:2 * IC]
        bias_ps = gu[0:B, 1, 1, 0:D]

        subj_in = sem("subj_in")
        cond_in = sem("cond_in")
        cond_in_pool = sem("cond_in_pool")
        bias_ld = sem("bias_ld")
        scale_ld = sem("scale_ld")
        down_sc_ld = sem("down_sc_ld")
        x_ld = [sem(f"x_ld{n}") for n in range(HALVES)]
        gu_ld = [sem(f"gu_ld{i}") for i in range(IC)]
        down_ld = [sem(f"down_ld{i}") for i in range(len(DOWN_LOADS))]
        warm_set = sem("warm_set")
        iota_made = sem("iota_made")
        ident_zeroed = sem("ident_zeroed")
        ident_made = sem("ident_made")
        ones_set = sem("ones_set")
        least_set = sem("least_set")
        bd_zeroed = sem("bd_zeroed")
        subj_float = sem("subj_float")
        subj_placed = sem("subj_placed")
        picks_made = sem("picks_made")
        bias_pick_made = sem("bias_pick_made")
        cond_picked = [sem(f"cond_picked{n}") for n in range(HALVES)]
        cond_placed = [sem(f"cond_placed{n}") for n in range(HALVES)]
        bias_picked = sem("bias_picked")
        bias_hi_made = sem("bias_hi_made")
        bias_lo_made = sem("bias_lo_made")
        bias_placed = sem("bias_placed")
        ones_made = sem("ones_made")
        scale_tp = sem("scale_tp")
        scales_made = sem("scales_made")
        h_made = sem("h_made")
        h_hi_made = sem("h_hi_made")
        h_lo_made = sem("h_lo_made")
        quant_power = sem("quant_power")
        quant_big = sem("quant_big")
        quant_sum = sem("quant_sum")
        quant_done = sem("quant_done")
        early_power = sem("early_power")
        early_big = sem("early_big")
        early_sum = sem("early_sum")
        early_done = sem("early_done")
        gate_made = sem("gate_made")
        up_made = sem("up_made")
        silu_made = sem("silu_made")
        fuse_made = sem("fuse_made")
        f_hi_made = sem("f_hi_made")
        f_lo_dve = sem("f_lo_dve")
        f_lo_pool = sem("f_lo_pool")
        f_lo_last = sem("f_lo_last")
        down_made = sem("down_made")
        y_made = sem("y_made")
        y_scaled = sem("y_scaled")
        res_dve = sem("res_dve")
        res_pool = sem("res_pool")
        stored = sem("stored")

        block = ctx.enter_context(nc.Block())

        def lo_wait(eng, s):
            eng.wait_ge((f_lo_dve, f_lo_pool)[s % 2], s // 2 + 1)

        @block.sync
        def _(sp):
            sp.dma_start(subj_i[:], subjects.partition_broadcast(P)).then_inc(subj_in, 16)
            for j in range(2, J - 1):
                sp.dma_start(cond_rep[j * C:(j + 1) * C], cond_rows).then_inc(cond_in, 16)
            sp.dma_start(x_sb[:, 0:GH], x_rows[:, 0:GH]).then_inc(x_ld[0], 16)

            def load_gu(i):
                for part, rows in ((0, gate_rows), (1, up_rows)):
                    dst = w_in[:, i, part * KC * P:(part + 1) * KC * P].rearrange("p (k c) -> p k c", k=KC)
                    sp.dma_start(dst, rows[:, :, i * P:(i + 1) * P]).then_inc(gu_ld[i], 16)

            def load_down(q):
                i0, i1 = DOWN_LOADS[q]
                sp.dma_start(w_in[:, i0:i1, GU:WCOL], down_rows[:, i0:i1]).then_inc(down_ld[q], 16)

            load_gu(0)
            sp.dma_start(x_sb[:, GH:G], x_rows[:, GH:G]).then_inc(x_ld[1], 16)
            load_down(0)
            load_gu(1)
            load_down(1)
            load_gu(2)
            load_down(2)
            for i in range(3, IC):
                load_gu(i)
            sp.dma_start(down_sc[:], down_scale.partition_broadcast(P)).then_inc(down_sc_ld, 16)
            sp.wait_ge(res_dve, GH // 2)
            sp.wait_ge(res_pool, GH // 2)
            sp.dma_start(out_rows[:, 0:GH], res[:, 0:GH]).then_inc(stored, 16)
            sp.wait_ge(res_dve, GH // 2 + 1)
            sp.wait_ge(res_pool, GH // 2 + 1)
            sp.dma_start(out_rows[:, GH:GH + 2], res[:, GH:GH + 2]).then_inc(stored, 16)
            sp.wait_ge(res_pool, GH // 2 + 2)
            sp.dma_start(out_rows[:, G - 2], res[:, G - 2]).then_inc(stored, 16)
            sp.wait_ge(stored, 16 * 4)

        @block.scalar
        def _(act):
            for j in range(0, 2):
                act.dma_start(cond_rep[j * C:(j + 1) * C], cond_rows).then_inc(cond_in, 16)
            act.dma_start(bias_in[:], bias).then_inc(bias_ld, 16)
            nc.scalar.preload_act_table(ACT.Silu)

            def big(i, hi=WCOL):
                act.wait_ge(quant_power, i + 1)
                nc.scalar.activation(w_big[:, i, 0:hi], w_big[:, i, 0:hi], ACT.Relu, bias=big_least[:],
                                     scale=SHIFT).then_inc(quant_big, 1)

            act.wait_ge(bias_picked, 1)
            nc.scalar.copy(bias_b[:, 0], bias_ps).then_inc(bias_hi_made, 1)
            def place(n):
                groups = slice(n * GH, (n + 1) * GH)
                act.wait_ge(cond_picked[n], N)
                for j in range(0, 2):
                    rows = slice(j * C, (j + 1) * C)
                    nc.scalar.copy(cond_bd[rows, groups, j * D:(j + 1) * D],
                                   cond_g[rows, groups]).then_inc(cond_placed[n], 1)

            act.wait_ge(bd_zeroed, 1)
            place(0)
            act.wait_ge(least_set, 1)
            big(0, GU)
            place(1)
            act.wait_ge(scale_tp, 1)
            nc.scalar.copy(scale_col[:], scale_ps).then_inc(scales_made, 1)
            for n in range(HALVES):
                for k in range(KC):
                    act.wait_ge(h_made, KC * n + k + 1)
                    nc.scalar.copy(h_hi[:, n, k], acc[:, KC * n + k]).then_inc(h_hi_made, 1)
                if n == 0:
                    big(1, GU)
            act.wait_ge(scales_made, 1)

            def silu_of(s):
                act.wait_ge(gate_made, s + 1)
                if s >= 2:
                    act.wait_ge(fuse_made, s - 1)
                i = STEP[s][0]
                nc.scalar.activation(silu[:, s % 2], gu[:, s % 2, 0], ACT.Silu,
                                     scale=scale_col[:, i:i + 1]).then_inc(silu_made, 1)

            def round_of(s, cols, count):
                act.wait_ge(fuse_made, count)
                if s >= SLOTS:
                    act.wait_ge(down_made, s - SLOTS + 1)
                nc.scalar.copy(f_hi[:, s % SLOTS, cols], fuse[:, s % SLOTS, cols]).then_inc(f_hi_made, 1)

            for s in range(STEPS):
                silu_of(s)
                if s >= 1:
                    round_of(s - 1, slice(0, TOK), s)
                if s % 2 == 0 and s // 2 + 2 < IC:
                    big(s // 2 + 2)
            for q in range(LAST):
                round_of(STEPS - 1, slice(q * TOK // LAST, (q + 1) * TOK // LAST), STEPS + q)
            act.wait_ge(res_dve, G // 2)
            act.dma_start(out_rows[:, G - 1], res[:, G - 1]).then_inc(stored, 16)

        @block.gpsimd
        def _(pool):
            pool.dma_start(cond_rep[(J - 1) * C:J * C], cond_rows).then_inc(cond_in_pool, 16)
            nc.gpsimd.iota(iota_n[:], [[1, N]], base=0, channel_multiplier=0,
                           allow_small_or_imprecise_dtypes=True).then_inc(iota_made, 1)
            pool.wait_ge(iota_made, 1)
            nc.gpsimd.iota(iota_p[:], [[0, 1]], base=0, channel_multiplier=1,
                           allow_small_or_imprecise_dtypes=True).then_inc(iota_made, 1)
            pool.wait_ge(iota_made, 2)
            nc.gpsimd.memset(ident[:], 0.0).then_inc(ident_zeroed, 1)
            pool.wait_ge(ident_zeroed, 1)
            nc.gpsimd.affine_select(out=ident[:], in_=ident[:], compare_op=ALU.not_equal, fill=1.0, base=0,
                                    pattern=[[-1, 2 * IC]], channel_multiplier=1).then_inc(ident_made, 1)
            pool.wait_ge(ident_made, 1)
            pool.dma_start(scale_in[0:IC], gate_scale.rearrange("(q p) -> q p", p=P)).then_inc(scale_ld, 16)
            pool.dma_start(scale_in[IC:2 * IC], up_scale.rearrange("(q p) -> q p", p=P)).then_inc(scale_ld, 16)
            nc.gpsimd.memset(cond_bd[:], 0.0).then_inc(bd_zeroed, 1)
            nc.gpsimd.memset(big_least[:], -LEAST * SHIFT).then_inc(least_set, 1)
            pool.wait_ge(bias_hi_made, 1)
            pool.dma_start(bias_tok[0:1].bitcast(F32), bias_b[:, 0].bitcast(F32)).then_inc(bias_placed, 16)
            pool.wait_ge(bias_lo_made, 1)
            pool.dma_start(bias_tok[1:2].bitcast(F32), bias_b[:, 1].bitcast(F32)).then_inc(bias_placed, 16)

            for i in range(EARLY):
                pool.wait_ge(early_big, i + 1)
                nc.gpsimd.tensor_tensor(w_in[:, i, GU:WCOL], w_in[:, i, GU:WCOL], w_big[:, i, GU:WCOL],
                                        ALU.add).then_inc(early_sum, 1)
                pool.wait_ge(early_sum, i + 1)
                nc.gpsimd.tensor_tensor(w_q[:, i, GU:WCOL], w_in[:, i, GU:WCOL], w_big[:, i, GU:WCOL],
                                        ALU.subtract).then_inc(early_done, 1)

            for s in range(1, STEPS - 1, 2):
                pool.wait_ge(f_hi_made, s + 1)
                if s >= SLOTS:
                    pool.wait_ge(down_made, s - SLOTS + 1)
                nc.gpsimd.tensor_tensor(f_lo[:, s % SLOTS], fuse[:, s % SLOTS],
                                        f_hi[:, s % SLOTS].bitcast(F32),
                                        ALU.subtract).then_inc(f_lo_pool, 1)

            for m in range(0, G, 2):
                pool.wait_ge(x_ld[m // GH], 16)
                pool.wait_ge(y_scaled, m + 1)
                nc.gpsimd.tensor_tensor(res[:, m], y_sc[:, m], x_sb[:, m], ALU.add).then_inc(res_pool, 1)

        @block.vector
        def _(dve):
            def power(i, hi=WCOL):
                dve.wait_ge(gu_ld[i], 32)
                if hi > GU:
                    dve.wait_ge(down_ld[min(i, len(DOWN_LOADS) - 1)], 16)
                nc.vector.tensor_scalar(w_big[:, i, 0:hi].bitcast(U32), w_in[:, i, 0:hi].bitcast(U32), EXPONENT,
                                        HALF_MORE, ALU.bitwise_and, ALU.bitwise_or).then_inc(quant_power, 1)

            def early_bigs(i):
                dve.wait_ge(down_ld[i], 16)
                nc.vector.tensor_scalar(w_big[:, i, GU:WCOL].bitcast(U32), w_in[:, i, GU:WCOL].bitcast(U32),
                                        EXPONENT, HALF_MORE, ALU.bitwise_and, ALU.bitwise_or
                                        ).then_inc(early_power, 1)
                dve.wait_ge(early_power, i + 1)
                nc.vector.tensor_scalar(w_big[:, i, GU:WCOL], w_big[:, i, GU:WCOL], LEAST, SHIFT,
                                        ALU.max, ALU.mult).then_inc(early_big, 1)

            def add_big(i, hi=WCOL):
                dve.wait_ge(quant_big, i + 1)
                nc.vector.scalar_tensor_tensor(w_in[:, i, 0:hi], w_big[:, i, 0:hi], LEAST * SHIFT,
                                               w_in[:, i, 0:hi], ALU.add, ALU.add).then_inc(quant_sum, 1)

            def take_big(i, hi=WCOL):
                dve.wait_ge(quant_sum, i + 1)
                nc.vector.scalar_tensor_tensor(w_q[:, i, 0:hi], w_in[:, i, 0:hi], LEAST * SHIFT,
                                               w_big[:, i, 0:hi], ALU.subtract, ALU.subtract
                                               ).then_inc(quant_done, 1)

            nc.vector.memset(warm[:].bitcast(U32), 0).then_inc(warm_set, 1)
            nc.vector.memset(ones_f[:], 1.0).then_inc(ones_set, 1)
            dve.wait_ge(ones_set, 1)
            nc.vector.tensor_copy(ones_r[:], ones_f[:]).then_inc(ones_made, 1)
            dve.wait_ge(subj_in, 16)
            nc.vector.tensor_copy(subj_f[:], subj_i[:]).then_inc(subj_float, 1)
            dve.wait_ge(subj_float, 1)
            dve.wait_ge(iota_made, 2)
            nc.vector.tensor_tensor(pick_b[:], subj_f[0:N], iota_p[:].to_broadcast([N, B]),
                                    ALU.is_equal).then_inc(bias_pick_made, 1)
            for j in range(J):
                rows = slice(j * C, (j + 1) * C)
                nc.vector.tensor_copy(subj_g[rows], subj_f[rows].rearrange("p (g j) -> p g j", j=J)[:, :, j]
                                      ).then_inc(subj_placed, 1)
            dve.wait_ge(subj_placed, J)
            nc.vector.tensor_tensor(pick[:], subj_g[:].unsqueeze(1).to_broadcast([P, N, G]),
                                    iota_n[:].unsqueeze(2).to_broadcast([P, N, G]),
                                    ALU.is_equal).then_inc(picks_made, 1)

            def pick_cond(h, n):
                groups = slice(h * GH, (h + 1) * GH)
                data = cond_rep[:, n].unsqueeze(1).to_broadcast([P, GH, D])
                if n == 0:
                    nc.vector.tensor_copy(cond_g[:, groups], data).then_inc(cond_picked[h], 1)
                else:
                    dve.wait_ge(cond_picked[h], n)
                    nc.vector.copy_predicated(cond_g[:, groups],
                                              pick[:, n, groups].unsqueeze(2).to_broadcast([P, GH, D]),
                                              data).then_inc(cond_picked[h], 1)

            def place(h):
                groups = slice(h * GH, (h + 1) * GH)
                dve.wait_ge(cond_picked[h], N)
                for j in range(2, J):
                    rows = slice(j * C, (j + 1) * C)
                    nc.vector.tensor_copy(cond_bd[rows, groups, j * D:(j + 1) * D],
                                          cond_g[rows, groups]).then_inc(cond_placed[h], 1)

            dve.wait_ge(picks_made, 1)
            dve.wait_ge(cond_in, 16 * (J - 1))
            dve.wait_ge(cond_in_pool, 16)
            for n in range(N):
                pick_cond(0, n)
                if n == N // 2:
                    dve.wait_ge(bias_hi_made, 1)
                    nc.vector.tensor_tensor(bias_b[:, 1], bias_ps, bias_b[:, 0].bitcast(F32),
                                            ALU.subtract).then_inc(bias_lo_made, 1)
            dve.wait_ge(bd_zeroed, 1)
            place(0)
            power(0, GU)
            for n in range(N):
                pick_cond(1, n)
                if n == N - 3:
                    add_big(0, GU)
            place(1)
            take_big(0, GU)
            power(1, GU)

            between = [lambda: early_bigs(0), lambda: early_bigs(1), lambda: add_big(1, GU), lambda: take_big(1, GU)]
            for n in range(HALVES):
                for k in range(KC):
                    dve.wait_ge(h_hi_made, KC * n + k + 1)
                    nc.vector.tensor_tensor(h_lo[:, n, k], acc[:, KC * n + k], h_hi[:, n, k].bitcast(F32),
                                            ALU.subtract).then_inc(h_lo_made, 1)
                    between[KC * n + k]()
            power(2)

            def fuse_of(s, cols):
                dve.wait_ge(up_made, s + 1)
                dve.wait_ge(silu_made, s + 1)
                if s >= SLOTS:
                    lo_wait(dve, s - SLOTS)
                i = STEP[s][0]
                nc.vector.scalar_tensor_tensor(
                    fuse[:, s % SLOTS, cols], gu[:, s % 2, 1, cols], scale_col[:, IC + i:IC + i + 1],
                    silu[:, s % 2, cols], ALU.mult, ALU.mult).then_inc(fuse_made, 1)

            def rest_of(s, cols, count):
                dve.wait_ge(f_hi_made, count)
                if s >= SLOTS:
                    dve.wait_ge(down_made, s - SLOTS + 1)
                nc.vector.tensor_tensor(f_lo[:, s % SLOTS, cols], fuse[:, s % SLOTS, cols],
                                        f_hi[:, s % SLOTS, cols].bitcast(F32),
                                        ALU.subtract).then_inc(f_lo_last if s == STEPS - 1 else f_lo_dve, 1)

            dve.wait_ge(scales_made, 1)
            whole = slice(0, TOK)
            def scale_y(m):
                nc.vector.tensor_tensor(y_sc[:, m], acc[:, m // 2, (m % 2) * T:(m % 2 + 1) * T], down_sc[:],
                                        ALU.mult).then_inc(y_scaled, 1)

            def add_x(m):
                dve.wait_ge(y_scaled, m + 1)
                nc.vector.tensor_tensor(res[:, m], y_sc[:, m], x_sb[:, m], ALU.add).then_inc(res_dve, 1)

            for s in range(STEPS - 1):
                i = s // 2 + 2
                fuse_of(s, whole)
                if i < IC:
                    if s % 2 == 0:
                        add_big(i)
                        if i + 1 < IC:
                            power(i + 1)
                    else:
                        take_big(i)
                if s % 2 == 1:
                    rest_of(s - 1, whole, s)
            dve.wait_ge(down_sc_ld, 16)
            for n in range(HALVES):
                dve.wait_ge(x_ld[n], 16)
            dve.wait_ge(down_made, HALF_DONE[0] + 1)
            for m in range(0, GH, 2):
                scale_y(m)
                scale_y(m + 1)
                add_x(m + 1)
            pieces = [slice(q * TOK // LAST, (q + 1) * TOK // LAST) for q in range(LAST)]

            fuse_of(STEPS - 1, pieces[0])
            rest_of(STEPS - 2, whole, STEPS - 1)
            for q in range(1, LAST):
                fuse_of(STEPS - 1, pieces[q])
            for q in range(LAST):
                rest_of(STEPS - 1, pieces[q], STEPS + q)

            for m in range(GH, G, 2):
                dve.wait_ge(y_made, m - GH + 2)
                scale_y(m)
                scale_y(m + 1)
                add_x(m + 1)

        @block.tensor
        def _(pe):
            pe.wait_ge(warm_set, 1)
            for _ in range(WARM[0]):
                nc.tensor.matmul(warm_ps, warm[:, 0:P], warm[:], start=True, stop=True)
            pe.wait_ge(bias_pick_made, 1)
            pe.wait_ge(bias_ld, 16)
            nc.tensor.matmul(bias_ps, pick_b[:], bias_in[:], start=True, stop=True).then_inc(bias_picked, 1)
            pe.wait_ge(ident_made, 1)
            pe.wait_ge(scale_ld, 32)
            nc.tensor.matmul(scale_ps, scale_in[:], ident[:], start=True, stop=True).then_inc(scale_tp, 1)
            for _ in range(WARM[1]):
                nc.tensor.matmul(warm_ps, warm[:, 0:P], warm[:], start=True, stop=True)

            for n in range(HALVES):
                pe.wait_ge(cond_placed[n], J)
                pe.wait_ge(x_ld[n], 16)
                for k in range(KC):
                    bank = acc[:, KC * n + k]
                    for g in range(GH):
                        nc.tensor.matmul(bank[:, g * P:(g + 1) * P], x_sb[:, n * GH + g, k * P:(k + 1) * P],
                                         cond_bd[:, n * GH + g], start=(g == 0), stop=False,
                                         skip_group_check=True)
                    if n == 0 and k == 0:
                        pe.wait_ge(ones_made, 1)
                        pe.wait_ge(bias_placed, 32)
                    nc.tensor.matmul(bank, ones_r[:], bias_tok[:, n * TOK // D:(n + 1) * TOK // D], start=False,
                                     stop=True, skip_group_check=True).then_inc(h_made, 1)

            def gate_up(s):
                i, n = STEP[s]
                if s >= 2:
                    pe.wait_ge(silu_made, s - 1)
                pe.wait_ge(quant_done, i + 1)
                for part, made in ((0, gate_made), (1, up_made)):
                    if part == 1 and s >= 2:
                        pe.wait_ge(fuse_made, s - 1)
                    if s == 1 and part == 0:
                        pe.wait_ge(scales_made, 1)
                    if s == 1 and part == 1:
                        pe.wait_ge(bias_lo_made, 1)
                    for v, (h, h_sem) in enumerate(((h_hi, h_hi_made), (h_lo, h_lo_made))):
                        for k in range(KC):
                            if s < 2 and part == 0:
                                pe.wait_ge(h_sem, KC * n + k + 1)
                            col = (part * KC + k) * P
                            last = nc.tensor.matmul(gu[:, s % 2, part], w_q[:, i, col:col + P], h[:, n, k],
                                                    start=(v == 0 and k == 0), stop=(v == 1 and k == KC - 1))
                    last.then_inc(made, 1)

            def down_tile(s, v, m):
                i, n = STEP[s]
                tile = n * GH + m
                return nc.tensor.matmul(acc[:, tile // 2, (tile % 2) * T:(tile % 2 + 1) * T],
                                        (f_hi, f_lo)[v][:, s % SLOTS, m * P:(m + 1) * P], w_q[:, i, GU:WCOL],
                                        start=(i == 0 and v == 0 and tile % 2 == 0),
                                        stop=(i == IC - 1 and v == 1), skip_group_check=True)

            def down(s):
                i, n = STEP[s]
                if i < EARLY:
                    pe.wait_ge(early_done, i + 1)
                if s < 2:
                    pe.wait_ge(h_lo_made, KC * (n + 1))
                pe.wait_ge(f_hi_made, s + 1)
                for m in range(GH):
                    down_tile(s, 0, m)
                lo_wait(pe, s)
                for m in range(GH):
                    last = down_tile(s, 1, m)
                last.then_inc(down_made, 1)

            for s in range(STEPS):
                gate_up(s)
                if s >= LAG:
                    down(s - LAG)
            down(STEPS - 2)
            for q in range(LAST):
                pe.wait_ge(f_hi_made, STEPS + q)
                for m in range(q * GH // LAST, (q + 1) * GH // LAST):
                    down_tile(STEPS - 1, 0, m)
                pe.wait_ge(f_lo_last, q + 1)
                for m in range(q * GH // LAST, (q + 1) * GH // LAST):
                    down_tile(STEPS - 1, 1, m).then_inc(y_made, 1)


_INS = ["x", "itok_B_0_7", "fside_8xS_0", "L0_cond_weights", "L0_ffn_gate_w", "L0_ffn_up_w", "L0_ffn_down_w",
        "L0_ffn_gate_scale", "L0_ffn_up_scale", "L0_ffn_down_scale"]


def kernel(**inputs):
    import numpy as _np
    import concourse.bacc as _bacc
    from concourse import mybir as _mybir
    from concourse.bass_utils import run_bass_kernel_spmd as _run

    nc = _bacc.Bacc("TRN2", target_bir_lowering=False, num_devices=1)
    arrays, args = {}, []
    for name in _INS:
        a = _np.ascontiguousarray(inputs[name])
        arrays[f"in_{name}_dram"] = a
        args.append(nc.dram_tensor(f"in_{name}_dram", a.shape, _mybir.dt.from_np(a.dtype), kind="ExternalInput").ap())
    shape = arrays["in_x_dram"].shape
    args.append(nc.dram_tensor("out_0_dram", shape, _mybir.dt.float32, kind="ExternalOutput").ap())
    adaln_ffn(nc, *args)
    r = _run(nc, [arrays], core_ids=[0])
    return r.results[0]["out_0_dram"]
```

```python
from contextlib import ExitStack

import concourse.bass as bass
from concourse import mybir

ALU = mybir.AluOpType
ACT = mybir.ActivationFunctionType
BF16 = mybir.dt.bfloat16
F32 = mybir.dt.float32
F32R = mybir.dt.float32r
I32 = mybir.dt.int32
U32 = mybir.dt.uint32

P = 128


def adaln_ffn(
    nc: bass.Bass,
    x: bass.AP,
    subjects: bass.AP,
    bias: bass.AP,
    cond_w: bass.AP,
    gate_w: bass.AP,
    up_w: bass.AP,
    down_w: bass.AP,
    gate_scale: bass.AP,
    up_scale: bass.AP,
    down_scale: bass.AP,
    out: bass.AP,
):
    B, C, T = x.shape
    N, _, D = cond_w.shape
    HID = gate_w.shape[1]
    J = P // C
    G = B // J
    KC = T // P
    IC = HID // P
    HALVES = 2
    TOK = B * D // HALVES
    GH = G // HALVES
    GATE = KC * P
    GU = 2 * KC * P
    WCOL = GU + T
    STEPS = IC * HALVES
    LAG = 2
    SLOTS = 4
    EARLY = ((0, GATE, GU), (1, 0, GU), (0, GU, WCOL), (1, GU, WCOL))
    LAST = 2
    GP = GH // 2
    LO_ROW = 32
    BR = LO_ROW + N
    WARM = (12, 1)
    DOWN_LOADS = ((0, 1), (1, 2), (2, IC))
    STEP = [(i, n) for i in range(IC - 3) for n in range(HALVES)] + [(i, n) for n in range(HALVES)
                                                                     for i in range(IC - 3, IC)]
    HALF_DONE = [max(s for s, (_, m) in enumerate(STEP) if m == n) for n in range(HALVES)]
    assert C == D and TOK == 512 and B * C == G * P

    EXPONENT = 0x7F800000
    HALF_MORE = 0x00400000
    LEAST = 1.5 * 2.0 ** -6
    SHIFT = 2.0 ** (23 - 3)

    x_rows = x.rearrange("(g j) c t -> (j c) g t", j=J)
    out_rows = out.rearrange("(g j) c t -> (j c) g t", j=J)
    cond_rows = cond_w.rearrange("n c d -> c n d")
    gate_rows = gate_w.rearrange("(k p) i -> p k i", p=P)
    up_rows = up_w.rearrange("(k p) i -> p k i", p=P)
    down_rows = down_w.rearrange("(q p) t -> p q t", p=P)

    with ExitStack() as ctx:
        def sb(name, shape, dt=F32):
            return ctx.enter_context(nc.sbuf_tensor(name, shape, dt))

        def ps(name, shape):
            return ctx.enter_context(nc.psum_tensor(name, shape, F32))

        def sem(name):
            return ctx.enter_context(nc.semaphore(name))

        x_sb = sb("x_sb", [P, G, T])
        subj_i = sb("subj_i", [P, B], I32)
        cond_rep = sb("cond_rep", [P, N, D])
        bias_in = sb("bias_in", [BR, D])
        scale_in = sb("scale_in", [2 * IC, P])
        scale_col = sb("scale_col", [P, 2 * IC])
        down_sc = sb("down_sc", [P, T])
        w_in = sb("w_in", [P, IC, WCOL])
        w_big = sb("w_big", [P, IC, WCOL])
        w_q = sb("w_q", [P, IC, WCOL], F32R)
        subj_f = sb("subj_f", [P, B])
        subj_g = sb("subj_g", [P, G])
        iota_n = sb("iota_n", [P, N])
        iota_p = sb("iota_p", [BR, 1])
        big_least = sb("big_least", [P, 1])
        ident = sb("ident", [2 * IC, 2 * IC])
        warm = sb("warm", [P, TOK], BF16)
        ones_f = sb("ones_f", [BR, P])
        ones_r = sb("ones_r", [BR, P], F32R)
        pick = sb("pick", [P, N, G], U32)
        pick_b = sb("pick_b", [BR, B])
        cond_g = sb("cond_g", [P, G, D])
        cond_bd = sb("cond_bd", [P, G, P])
        bias_r = sb("bias_r", [BR, D], F32R)
        bias_tok = sb("bias_tok", [BR, B, D], F32R)
        h_hi = sb("h_hi", [P, HALVES, KC, TOK], F32R)
        h_lo = sb("h_lo", [P, HALVES, KC, TOK], F32R)
        silu = sb("silu", [P, 2, TOK])
        fuse = sb("fuse", [P, SLOTS, TOK])
        f_hi = sb("f_hi", [P, SLOTS, TOK], F32R)
        f_lo = sb("f_lo", [P, SLOTS, TOK], F32R)
        y_sc = sb("y_sc", [P, G, T])
        res = sb("res", [P, G, T])

        acc = ps("acc", [P, 4, 512])
        gu = ps("gu", [P, 2, 2, 512])
        warm_ps = gu[:, 0, 0]
        scale_ps = gu[:, 1, 0, 0:2 * IC]

        subj_in = sem("subj_in")
        cond_in = sem("cond_in")
        cond_in_pool = sem("cond_in_pool")
        bias_zeroed = sem("bias_zeroed")
        bias_ld = [sem(f"bias_ld{part}") for part in range(2)]
        scale_ld = sem("scale_ld")
        down_sc_ld = sem("down_sc_ld")
        x_ld = [sem(f"x_ld{n}") for n in range(HALVES)]
        gu_ld = [sem(f"gu_ld{i}") for i in range(IC)]
        down_ld = [sem(f"down_ld{i}") for i in range(len(DOWN_LOADS))]
        warm_set = sem("warm_set")
        iota_made = sem("iota_made")
        ident_zeroed = sem("ident_zeroed")
        ident_made = sem("ident_made")
        ones_set = sem("ones_set")
        least_set = sem("least_set")
        bd_zeroed = sem("bd_zeroed")
        subj_float = sem("subj_float")
        subj_placed = sem("subj_placed")
        picks_made = sem("picks_made")
        bias_pick_made = sem("bias_pick_made")
        cond_first = [sem(f"cond_first{q}") for q in range(G // GP)]
        cond_picked = [sem(f"cond_picked{q}") for q in range(G // GP)]
        cond_placed = [sem(f"cond_placed{n}") for n in range(HALVES)]
        bias_hi_made = sem("bias_hi_made")
        bias_lo_made = sem("bias_lo_made")
        bias_placed = sem("bias_placed")
        ones_made = sem("ones_made")
        scale_tp = sem("scale_tp")
        scales_made = sem("scales_made")
        h_made = sem("h_made")
        h_hi_made = sem("h_hi_made")
        h_lo_made = sem("h_lo_made")
        quant_power = sem("quant_power")
        quant_big = sem("quant_big")
        quant_sum = sem("quant_sum")
        quant_done = sem("quant_done")
        early_power = sem("early_power")
        early_big = sem("early_big")
        early_sum = sem("early_sum")
        early_done = sem("early_done")
        gate_made = sem("gate_made")
        up_made = sem("up_made")
        silu_made = sem("silu_made")
        fuse_made = sem("fuse_made")
        f_hi_made = sem("f_hi_made")
        f_lo_first = sem("f_lo_first")
        f_lo_pool = sem("f_lo_pool")
        f_lo_last = sem("f_lo_last")
        down_made = sem("down_made")
        y_made = sem("y_made")
        y_scaled = sem("y_scaled")
        res_dve = sem("res_dve")
        res_pool = sem("res_pool")
        stored = sem("stored")

        block = ctx.enter_context(nc.Block())

        def quantised(i):
            return i + 1 - (i >= 1)

        def lo_wait(eng, s):
            if s == 0:
                eng.wait_ge(f_lo_first, 1)
            else:
                eng.wait_ge(f_lo_pool, s)

        @block.sync
        def _(sp):
            sp.dma_start(subj_i[:], subjects.partition_broadcast(P)).then_inc(subj_in, 16)
            for j in range(2, J - 1):
                sp.dma_start(cond_rep[j * C:(j + 1) * C], cond_rows).then_inc(cond_in, 16)
            sp.wait_ge(bias_zeroed, 1)
            sp.dma_start(bias_in[LO_ROW:BR], bias).then_inc(bias_ld[1], 16)
            sp.dma_start(x_sb[:, 0:GH], x_rows[:, 0:GH]).then_inc(x_ld[0], 16)

            def load_gu(i):
                for part, rows in ((0, gate_rows), (1, up_rows)):
                    dst = w_in[:, i, part * KC * P:(part + 1) * KC * P].rearrange("p (k c) -> p k c", k=KC)
                    sp.dma_start(dst, rows[:, :, i * P:(i + 1) * P]).then_inc(gu_ld[i], 16)

            def load_down(q):
                i0, i1 = DOWN_LOADS[q]
                sp.dma_start(w_in[:, i0:i1, GU:WCOL], down_rows[:, i0:i1]).then_inc(down_ld[q], 16)

            load_gu(0)
            load_gu(1)
            sp.dma_start(x_sb[:, GH:G], x_rows[:, GH:G]).then_inc(x_ld[1], 16)
            for part, scale in ((0, gate_scale), (1, up_scale)):
                sp.dma_start(scale_in[part * IC:(part + 1) * IC],
                             scale.rearrange("(q p) -> q p", p=P)).then_inc(scale_ld, 16)
            load_down(0)
            load_down(1)
            load_gu(2)
            load_down(2)
            for i in range(3, IC):
                load_gu(i)
            sp.dma_start(down_sc[:], down_scale.partition_broadcast(P)).then_inc(down_sc_ld, 16)
            for m0, m1, pool_tiles, dve_tiles in ((0, 2, 1, 1), (2, 4, 2, 2), (4, 5, 3, 2), (5, 7, 4, 3), (7, 8, 4, 4)):
                sp.wait_ge(res_pool, pool_tiles)
                sp.wait_ge(res_dve, dve_tiles)
                sp.dma_start(out_rows[:, m0:m1], res[:, m0:m1]).then_inc(stored, 16)
            sp.wait_ge(stored, 16 * 5)

        @block.scalar
        def _(act):
            for j in range(0, 2):
                act.dma_start(cond_rep[j * C:(j + 1) * C], cond_rows).then_inc(cond_in, 16)

            def big(i, hi=WCOL):
                act.wait_ge(quant_power, quantised(i))
                nc.scalar.activation(w_big[:, i, 0:hi], w_big[:, i, 0:hi], ACT.Relu, bias=big_least[:],
                                     scale=SHIFT).then_inc(quant_big, 1)

            nc.scalar.preload_act_table(ACT.Silu)
            for part in range(2):
                act.wait_ge(bias_ld[part], 16)
            nc.scalar.copy(bias_r[:], bias_in[:]).then_inc(bias_hi_made, 1)
            act.wait_ge(cond_in, 16 * (J - 1))
            act.wait_ge(cond_in_pool, 16)
            for q in range(GH // GP, G // GP):
                nc.scalar.copy(cond_g[:, q * GP:(q + 1) * GP],
                               cond_rep[:, 0].unsqueeze(1).to_broadcast([P, GP, D])).then_inc(cond_first[q], 1)

            def place(n):
                groups = slice(n * GH, (n + 1) * GH)
                for q in range(n * GH // GP, (n + 1) * GH // GP):
                    act.wait_ge(cond_picked[q], N - 1)
                for j in range(0, 2):
                    rows = slice(j * C, (j + 1) * C)
                    nc.scalar.copy(cond_bd[rows, groups, j * D:(j + 1) * D],
                                   cond_g[rows, groups]).then_inc(cond_placed[n], 1)

            act.wait_ge(bd_zeroed, 1)
            place(0)
            act.wait_ge(least_set, 1)
            place(1)
            big(0, GATE)
            for n in range(HALVES):
                for k in range(KC):
                    act.wait_ge(h_made, KC * n + k + 1)
                    nc.scalar.copy(h_hi[:, n, k], acc[:, KC * n + k]).then_inc(h_hi_made, 1)
            act.wait_ge(scale_tp, 1)
            nc.scalar.copy(scale_col[:], scale_ps).then_inc(scales_made, 1)
            act.wait_ge(scales_made, 1)

            def silu_of(s):
                act.wait_ge(gate_made, s + 1)
                if s >= 2:
                    act.wait_ge(fuse_made, s - 1)
                i = STEP[s][0]
                nc.scalar.activation(silu[:, s % 2], gu[:, s % 2, 0], ACT.Silu,
                                     scale=scale_col[:, i:i + 1]).then_inc(silu_made, 1)

            def round_of(s, cols, count):
                act.wait_ge(fuse_made, count)
                if s >= SLOTS:
                    act.wait_ge(down_made, s - SLOTS + 1)
                nc.scalar.copy(f_hi[:, s % SLOTS, cols], fuse[:, s % SLOTS, cols]).then_inc(f_hi_made, 1)

            for s in range(STEPS):
                silu_of(s)
                if s == 1:
                    big(2)
                elif 3 <= s < IC:
                    big(s)
                if s < STEPS - 1:
                    round_of(s, slice(0, TOK), s + 1)
            for q in range(LAST):
                round_of(STEPS - 1, slice(q * TOK // LAST, (q + 1) * TOK // LAST), STEPS + q)

        @block.gpsimd
        def _(pool):
            pool.dma_start(cond_rep[(J - 1) * C:J * C], cond_rows).then_inc(cond_in_pool, 16)
            pool.wait_ge(bias_zeroed, 1)
            pool.dma_start(bias_in[0:N], bias).then_inc(bias_ld[0], 16)
            nc.gpsimd.iota(iota_p[0:LO_ROW], [[0, 1]], base=0, channel_multiplier=1,
                           allow_small_or_imprecise_dtypes=True).then_inc(iota_made, 1)
            pool.wait_ge(iota_made, 1)
            nc.gpsimd.iota(iota_p[LO_ROW:BR], [[0, 1]], base=0, channel_multiplier=1,
                           allow_small_or_imprecise_dtypes=True).then_inc(iota_made, 1)
            pool.wait_ge(iota_made, 2)
            nc.gpsimd.iota(iota_n[:], [[1, N]], base=0, channel_multiplier=0,
                           allow_small_or_imprecise_dtypes=True).then_inc(iota_made, 1)
            pool.wait_ge(iota_made, 3)
            nc.gpsimd.memset(ident[:], 0.0).then_inc(ident_zeroed, 1)
            pool.wait_ge(ident_zeroed, 1)
            nc.gpsimd.affine_select(out=ident[:], in_=ident[:], compare_op=ALU.not_equal, fill=1.0, base=0,
                                    pattern=[[-1, 2 * IC]], channel_multiplier=1).then_inc(ident_made, 1)
            pool.wait_ge(ident_made, 1)
            pool.wait_ge(bias_pick_made, 1)
            pool.wait_ge(bias_hi_made, 1)
            nc.gpsimd.tensor_tensor(bias_r[LO_ROW:BR], bias_in[LO_ROW:BR], bias_r[LO_ROW:BR].bitcast(F32),
                                    ALU.subtract).then_inc(bias_lo_made, 1)
            pool.wait_ge(bias_lo_made, 1)
            for n in range(HALVES):
                batches = slice(n * TOK // D, (n + 1) * TOK // D)
                shape = [BR, TOK // D, D]
                nc.gpsimd.tensor_tensor(bias_tok[:, batches], pick_b[:, batches].unsqueeze(2).to_broadcast(shape),
                                        bias_r[:].bitcast(F32).unsqueeze(1).to_broadcast(shape),
                                        ALU.mult).then_inc(bias_placed, 1)

            pool.wait_ge(bias_placed, HALVES)
            for e, (i, lo, hi) in enumerate(EARLY):
                pool.wait_ge(early_big, e + 1)
                nc.gpsimd.tensor_tensor(w_in[:, i, lo:hi], w_in[:, i, lo:hi], w_big[:, i, lo:hi],
                                        ALU.add).then_inc(early_sum, 1)
                pool.wait_ge(early_sum, e + 1)
                nc.gpsimd.tensor_tensor(w_q[:, i, lo:hi], w_in[:, i, lo:hi], w_big[:, i, lo:hi],
                                        ALU.subtract).then_inc(early_done, 1)

            for s in range(1, STEPS - 1):
                pool.wait_ge(f_hi_made, s + 1)
                if s >= SLOTS:
                    pool.wait_ge(down_made, s - SLOTS + 1)
                nc.gpsimd.tensor_tensor(f_lo[:, s % SLOTS], fuse[:, s % SLOTS],
                                        f_hi[:, s % SLOTS].bitcast(F32),
                                        ALU.subtract).then_inc(f_lo_pool, 1)

            for m, scaled in ((1, 1), (2, 2), (4, 3), (5, 4)):
                pool.wait_ge(x_ld[m // GH], 16)
                pool.wait_ge(y_scaled, scaled)
                nc.gpsimd.tensor_tensor(res[:, m], y_sc[:, m], x_sb[:, m], ALU.add).then_inc(res_pool, 1)

        @block.vector
        def _(dve):
            def power(i, hi=WCOL):
                dve.wait_ge(gu_ld[i], 32)
                if hi > GU:
                    dve.wait_ge(down_ld[min(i, len(DOWN_LOADS) - 1)], 16)
                nc.vector.tensor_scalar(w_big[:, i, 0:hi].bitcast(U32), w_in[:, i, 0:hi].bitcast(U32), EXPONENT,
                                        HALF_MORE, ALU.bitwise_and, ALU.bitwise_or).then_inc(quant_power, 1)

            def early_powers(e):
                i, lo, hi = EARLY[e]
                if lo < GU:
                    dve.wait_ge(gu_ld[i], 32)
                else:
                    dve.wait_ge(down_ld[i], 16)
                nc.vector.tensor_scalar(w_big[:, i, lo:hi].bitcast(U32), w_in[:, i, lo:hi].bitcast(U32),
                                        EXPONENT, HALF_MORE, ALU.bitwise_and, ALU.bitwise_or
                                        ).then_inc(early_power, 1)

            def early_bigs(e):
                i, lo, hi = EARLY[e]
                dve.wait_ge(early_power, e + 1)
                nc.vector.tensor_scalar(w_big[:, i, lo:hi], w_big[:, i, lo:hi], LEAST, SHIFT,
                                        ALU.max, ALU.mult).then_inc(early_big, 1)

            def add_big(i, hi=WCOL):
                dve.wait_ge(quant_big, quantised(i))
                nc.vector.scalar_tensor_tensor(w_in[:, i, 0:hi], w_big[:, i, 0:hi], LEAST * SHIFT,
                                               w_in[:, i, 0:hi], ALU.add, ALU.add).then_inc(quant_sum, 1)

            def take_big(i, hi=WCOL):
                dve.wait_ge(quant_sum, quantised(i))
                nc.vector.scalar_tensor_tensor(w_q[:, i, 0:hi], w_in[:, i, 0:hi], LEAST * SHIFT,
                                               w_big[:, i, 0:hi], ALU.subtract, ALU.subtract
                                               ).then_inc(quant_done, 1)

            nc.vector.memset(warm[:].bitcast(U32), 0).then_inc(warm_set, 1)
            nc.vector.memset(bias_in[:], 0.0).then_inc(bias_zeroed, 1)
            nc.vector.memset(ones_f[:], 1.0).then_inc(ones_set, 1)
            nc.vector.memset(big_least[:], -LEAST * SHIFT).then_inc(least_set, 1)
            nc.vector.memset(cond_bd[:], 0.0).then_inc(bd_zeroed, 1)
            dve.wait_ge(ones_set, 1)
            nc.vector.tensor_copy(ones_r[:], ones_f[:]).then_inc(ones_made, 1)
            dve.wait_ge(subj_in, 16)
            nc.vector.tensor_copy(subj_f[:], subj_i[:]).then_inc(subj_float, 1)
            dve.wait_ge(subj_float, 1)
            dve.wait_ge(iota_made, 2)
            nc.vector.tensor_tensor(pick_b[:], subj_f[0:BR], iota_p[:].to_broadcast([BR, B]),
                                    ALU.is_equal).then_inc(bias_pick_made, 1)
            for j in range(J):
                rows = slice(j * C, (j + 1) * C)
                nc.vector.tensor_copy(subj_g[rows], subj_f[rows].rearrange("p (g j) -> p g j", j=J)[:, :, j]
                                      ).then_inc(subj_placed, 1)
            dve.wait_ge(subj_placed, J)
            dve.wait_ge(iota_made, 3)
            nc.vector.tensor_tensor(pick[:], subj_g[:].unsqueeze(1).to_broadcast([P, N, G]),
                                    iota_n[:].unsqueeze(2).to_broadcast([P, N, G]),
                                    ALU.is_equal).then_inc(picks_made, 1)

            def pick_cond(q, n):
                groups = slice(q * GP, (q + 1) * GP)
                data = cond_rep[:, n].unsqueeze(1).to_broadcast([P, GP, D])
                if n == 0:
                    nc.vector.tensor_copy(cond_g[:, groups], data).then_inc(cond_first[q], 1)
                else:
                    if n == 1:
                        dve.wait_ge(cond_first[q], 1)
                    else:
                        dve.wait_ge(cond_picked[q], n - 1)
                    nc.vector.copy_predicated(cond_g[:, groups],
                                              pick[:, n, groups].unsqueeze(2).to_broadcast([P, GP, D]),
                                              data).then_inc(cond_picked[q], 1)

            def place(h):
                groups = slice(h * GH, (h + 1) * GH)
                for q in range(h * GH // GP, (h + 1) * GH // GP):
                    dve.wait_ge(cond_picked[q], N - 1)
                for j in range(2, J):
                    rows = slice(j * C, (j + 1) * C)
                    nc.vector.tensor_copy(cond_bd[rows, groups, j * D:(j + 1) * D],
                                          cond_g[rows, groups]).then_inc(cond_placed[h], 1)

            dve.wait_ge(picks_made, 1)
            dve.wait_ge(cond_in, 16 * (J - 1))
            dve.wait_ge(cond_in_pool, 16)
            for h in range(HALVES):
                for n in range(h, N):
                    for q in range(h * GH // GP, (h + 1) * GH // GP):
                        pick_cond(q, n)
                if h == 0:
                    dve.wait_ge(bd_zeroed, 1)
                    place(0)
            power(0, GATE)
            place(1)
            early_powers(0)
            early_powers(1)
            early_bigs(0)
            add_big(0, GATE)
            early_bigs(1)
            take_big(0, GATE)

            for n in range(HALVES):
                for k in range(KC):
                    dve.wait_ge(h_hi_made, KC * n + k + 1)
                    nc.vector.tensor_tensor(h_lo[:, n, k], acc[:, KC * n + k], h_hi[:, n, k].bitcast(F32),
                                            ALU.subtract).then_inc(h_lo_made, 1)
            early_powers(2)
            early_powers(3)
            early_bigs(2)

            def fuse_of(s, cols):
                dve.wait_ge(up_made, s + 1)
                dve.wait_ge(silu_made, s + 1)
                if s >= SLOTS:
                    lo_wait(dve, s - SLOTS)
                i = STEP[s][0]
                nc.vector.scalar_tensor_tensor(
                    fuse[:, s % SLOTS, cols], gu[:, s % 2, 1, cols], scale_col[:, IC + i:IC + i + 1],
                    silu[:, s % 2, cols], ALU.mult, ALU.mult).then_inc(fuse_made, 1)

            def rest_of(s, cols, count):
                dve.wait_ge(f_hi_made, count)
                if s >= SLOTS:
                    dve.wait_ge(down_made, s - SLOTS + 1)
                nc.vector.tensor_tensor(f_lo[:, s % SLOTS, cols], fuse[:, s % SLOTS, cols],
                                        f_hi[:, s % SLOTS, cols].bitcast(F32),
                                        ALU.subtract).then_inc(f_lo_last if s == STEPS - 1 else f_lo_first, 1)

            def scale_y(m0, m1):
                col = (m0 % 2) * T
                nc.vector.tensor_tensor(y_sc[:, m0:m1],
                                        acc[:, m0 // 2, col:col + (m1 - m0) * T].rearrange("p (m t) -> p m t", t=T),
                                        down_sc[:].unsqueeze(1).to_broadcast([P, m1 - m0, T]),
                                        ALU.mult).then_inc(y_scaled, 1)

            def add_x(m, count):
                dve.wait_ge(y_scaled, count)
                nc.vector.tensor_tensor(res[:, m], y_sc[:, m], x_sb[:, m], ALU.add).then_inc(res_dve, 1)

            dve.wait_ge(scales_made, 1)
            whole = slice(0, TOK)
            for s in range(STEPS - 1):
                fuse_of(s, whole)
                if s == 0:
                    early_bigs(3)
                    power(2)
                    rest_of(0, whole, 1)
                elif s == 1:
                    add_big(2)
                elif s == 2:
                    take_big(2)
                    power(3)
                elif s == 3:
                    power(4)
                    add_big(3)
                elif s == 4:
                    take_big(3)
                    power(5)
                elif s == 5:
                    add_big(4)
                    take_big(4)
                    add_big(5)
                elif s == 6:
                    take_big(5)
            dve.wait_ge(down_sc_ld, 16)
            for n in range(HALVES):
                dve.wait_ge(x_ld[n], 16)
            dve.wait_ge(down_made, HALF_DONE[0] + 1)
            scale_y(0, 2)
            scale_y(2, 4)
            add_x(0, 1)
            pieces = [slice(q * TOK // LAST, (q + 1) * TOK // LAST) for q in range(LAST)]
            for q in range(LAST):
                fuse_of(STEPS - 1, pieces[q])
            for q in range(LAST):
                rest_of(STEPS - 1, pieces[q], STEPS + q)
            add_x(3, 2)
            dve.wait_ge(y_made, 2)
            scale_y(4, 5)
            scale_y(5, 6)
            dve.wait_ge(y_made, 4)
            scale_y(6, 8)
            add_x(6, 5)
            add_x(7, 5)

        @block.tensor
        def _(pe):
            pe.wait_ge(warm_set, 1)
            for _ in range(WARM[0]):
                nc.tensor.matmul(warm_ps, warm[:, 0:P], warm[:], start=True, stop=True)

            for n in range(HALVES):
                pe.wait_ge(ones_made, 1)
                pe.wait_ge(bias_placed, n + 1)
                for k in range(KC):
                    nc.tensor.matmul(acc[:, KC * n + k], ones_r[:], bias_tok[:, n * TOK // D:(n + 1) * TOK // D],
                                     start=True, stop=False, skip_group_check=True)
                if n == 0:
                    for _ in range(WARM[1]):
                        nc.tensor.matmul(warm_ps, warm[:, 0:P], warm[:], start=True, stop=True)
                if n == 1:
                    pe.wait_ge(ident_made, 1)
                    pe.wait_ge(scale_ld, 32)
                    nc.tensor.matmul(scale_ps, scale_in[:], ident[:], start=True, stop=True).then_inc(scale_tp, 1)
                pe.wait_ge(cond_placed[n], J)
                pe.wait_ge(x_ld[n], 16)
                for k in range(KC):
                    bank = acc[:, KC * n + k]
                    for g in range(GH):
                        last = nc.tensor.matmul(bank[:, g * P:(g + 1) * P], x_sb[:, n * GH + g, k * P:(k + 1) * P],
                                                cond_bd[:, n * GH + g], start=False, stop=True,
                                                skip_group_check=True)
                    last.then_inc(h_made, 1)

            GU_ORDER = (((0, 0), (1, 0), (0, 1), (1, 1)), ((0, 0), (0, 1), (1, 0), (1, 1)))

            def gate_up(s):
                i, n = STEP[s]
                if s >= 2:
                    pe.wait_ge(silu_made, s - 1)
                if i == 1:
                    pe.wait_ge(early_done, 2)
                else:
                    pe.wait_ge(quant_done, quantised(i))
                for v, part in GU_ORDER[s < 2]:
                    h, h_sem = ((h_hi, h_hi_made), (h_lo, h_lo_made))[v]
                    if part == 1 and v == 0 and i == 0:
                        pe.wait_ge(early_done, 1)
                    if part == 1 and v == 0 and s >= 2:
                        pe.wait_ge(fuse_made, s - 1)
                    if s == 1 and part == 0 and v == 0:
                        pe.wait_ge(scales_made, 1)
                    for k in range(KC):
                        if s < 2 and part == 0:
                            pe.wait_ge(h_sem, KC * n + k + 1)
                        col = (part * KC + k) * P
                        last = nc.tensor.matmul(gu[:, s % 2, part], w_q[:, i, col:col + P], h[:, n, k],
                                                start=(v == 0 and k == 0), stop=(v == 1 and k == KC - 1))
                    if v == 1:
                        last.then_inc((gate_made, up_made)[part], 1)

            def down_tile(s, v, m):
                i, n = STEP[s]
                tile = n * GH + m
                return nc.tensor.matmul(acc[:, tile // 2, (tile % 2) * T:(tile % 2 + 1) * T],
                                        (f_hi, f_lo)[v][:, s % SLOTS, m * P:(m + 1) * P], w_q[:, i, GU:WCOL],
                                        start=(i == 0 and v == 0 and tile % 2 == 0),
                                        stop=(i == IC - 1 and v == 1), skip_group_check=True)

            def down(s):
                i, n = STEP[s]
                if i < 2:
                    pe.wait_ge(early_done, i + 3)
                if s < 2:
                    pe.wait_ge(h_lo_made, KC * (n + 1))
                pe.wait_ge(f_hi_made, s + 1)
                for m in range(GH):
                    down_tile(s, 0, m)
                lo_wait(pe, s)
                for m in range(GH):
                    last = down_tile(s, 1, m)
                last.then_inc(down_made, 1)

            for s in range(STEPS):
                gate_up(s)
                if s >= LAG:
                    down(s - LAG)
            down(STEPS - 2)
            for q in range(LAST):
                pe.wait_ge(f_hi_made, STEPS + q)
                for m in range(q * GH // LAST, (q + 1) * GH // LAST):
                    down_tile(STEPS - 1, 0, m)
                pe.wait_ge(f_lo_last, q + 1)
                for m in range(q * GH // LAST, (q + 1) * GH // LAST):
                    down_tile(STEPS - 1, 1, m).then_inc(y_made, 1)


_INS = ["x", "itok_B_0_7", "fside_8xS_0", "L0_cond_weights", "L0_ffn_gate_w", "L0_ffn_up_w", "L0_ffn_down_w",
        "L0_ffn_gate_scale", "L0_ffn_up_scale", "L0_ffn_down_scale"]


def kernel(**inputs):
    import numpy as _np
    import concourse.bacc as _bacc
    from concourse import mybir as _mybir
    from concourse.bass_utils import run_bass_kernel_spmd as _run

    nc = _bacc.Bacc("TRN2", target_bir_lowering=False, num_devices=1)
    arrays, args = {}, []
    for name in _INS:
        a = _np.ascontiguousarray(inputs[name])
        arrays[f"in_{name}_dram"] = a
        args.append(nc.dram_tensor(f"in_{name}_dram", a.shape, _mybir.dt.from_np(a.dtype), kind="ExternalInput").ap())
    shape = arrays["in_x_dram"].shape
    args.append(nc.dram_tensor("out_0_dram", shape, _mybir.dt.float32, kind="ExternalOutput").ap())
    adaln_ffn(nc, *args)
    r = _run(nc, [arrays], core_ids=[0])
    return r.results[0]["out_0_dram"]
```
